# Optimizing a Trainium2 kernel written in Bass

```python
import numpy as np
import jax
import jax.numpy as jnp

def _softmax(x, axis=-1):
    return jax.nn.softmax(x, axis=axis)
def _gelu(x):
    return jax.nn.gelu(x, approximate=True)
def _silu(x):
    return jax.nn.silu(x)
def _sigmoid(x):
    return jax.nn.sigmoid(x)
def _layernorm(x, axis=-1, eps=1e-5):
    m = jnp.mean(x, axis=axis, keepdims=True)
    v = jnp.var(x, axis=axis, keepdims=True)
    return (x - m) / jnp.sqrt(v + eps)
def _scatter_add(tgt, idx, src, axis=0):
    return tgt.at[idx].add(src)
def _segment_sum(src, seg, n):
    return jax.ops.segment_sum(src, seg, n)

kernel_name = 'mk_adj_resnorm_d2_adj_256_b71803'

def setup_inputs(seed: int = 0):
    np.random.seed(seed)
    _w = jnp.asarray
    def _rec_inputs():
        import jax
        import jax.numpy as jnp
        _gk = jax.random.key(seed)
        x = -0.000929 + 1 * jax.random.normal(jax.random.fold_in(_gk, 1), (8192, 256), jnp.float32)
        _a = jax.random.bernoulli(jax.random.fold_in(_gk, 2), 0.00195312, (8192, 8192))
        _a = jnp.logical_or(_a, jnp.swapaxes(_a, -1, -2))
        _a = jnp.logical_or(_a, jnp.eye(8192, dtype=bool))
        _af = _a.astype(jnp.float32)
        _af = _af * jax.random.uniform(jax.random.fold_in(_gk, 3), (8192, 8192), jnp.float32, 0.05, 5.41998)
        adj = _af
        return x, adj
    x, adj = _rec_inputs()
    def _L0_gnn_setup():
        import jax, jax.numpy as jnp
        import numpy as np
        N = 4096
        IN_DIM = 256
        H = 4
        D = 64
        NEG_SLOPE = 0.2
        key = jax.random.key(seed)
        k_h, k_adj, k_zero, k_W, k_a = jax.random.split(key, 5)
        h = jax.random.normal(k_h, (N, IN_DIM), dtype=jnp.float32)
        adj = jax.random.normal(k_adj, (N, N), dtype=jnp.float32)
        keep = jax.random.uniform(k_zero, (N, N)) >= 0.3
        adj_bias = jnp.where(keep, adj, 0.0)
        W = jax.random.normal(k_W, (IN_DIM, H * D), dtype=jnp.float32) * 0.05
        a = jax.random.normal(k_a, (H, 2 * D), dtype=jnp.float32) * 0.05
        return {'h': h, 'adj_bias': adj_bias, 'W': W, 'a': a}
    _L0_gnn_all = _L0_gnn_setup()
    _L0_gnn_in = {k: v for k, v in _L0_gnn_all.items() if k in ('W', 'a', )}
    del _L0_gnn_all

    def _L1_gnn_setup():
        import jax, jax.numpy as jnp
        import numpy as np
        N = 8192
        D = 256
        DENSITY = 0.02
        key = jax.random.key(seed)
        k1, k2, k3, k4 = jax.random.split(key, 4)
        inputs = jax.random.normal(k1, (N, D), dtype=jnp.float32)
        vals = jax.random.uniform(k2, (N, N), dtype=jnp.float32, minval=0.1, maxval=1.0)
        mask = jax.random.uniform(k3, (N, N), dtype=jnp.float32) < DENSITY
        adj = jnp.where(mask, vals, 0.0)
        H_v = 0.1 * jax.random.normal(k4, (D, 1), dtype=jnp.float32)
        return {'inputs': inputs, 'adj': adj, 'H_v': H_v}
    _L1_gnn_all = _L1_gnn_setup()
    _L1_gnn_in = {k: v for k, v in _L1_gnn_all.items() if k in ('H_v', )}
    del _L1_gnn_all

    return {
        "x": x,
        "adj": adj,
        "L0_gnn_W": _L0_gnn_in["W"],
        "L0_gnn_a": _L0_gnn_in["a"],
        "L1_gnn_H_v": _L1_gnn_in["H_v"],
    }

def reference(x, adj, L0_gnn_W, L0_gnn_a, L1_gnn_H_v):
    import jax
    import jax.numpy as jnp
    def _L0_gnn_ref(h, adj_bias, W, a):
        import jax, jax.numpy as jnp
        import numpy as np
        N = 4096
        IN_DIM = 256
        H = 4
        D = 64
        NEG_SLOPE = 0.2
        n = h.shape[0]
        Wh = (h @ W).reshape(n, H, D)
        a_i, a_j = (a[:, :D], a[:, D:])
        e_i = jnp.einsum('nhd,hd->nh', Wh, a_i)
        e_j = jnp.einsum('nhd,hd->nh', Wh, a_j)
        e = jax.nn.leaky_relu(e_i[:, None, :] + e_j[None, :, :], NEG_SLOPE)
        mask = (adj_bias == 0.0)[:, :, None]
        e = e + adj_bias[:, :, None]
        e = jnp.where(mask, -jnp.inf, e)
        all_masked = jnp.all(mask, axis=1, keepdims=True)
        self_loop = jnp.eye(n, dtype=bool)[:, :, None]
        e = jnp.where(all_masked & self_loop, 0.0, e)
        alpha = jax.nn.softmax(e, axis=1)
        out = jnp.einsum('ijh,jhd->ihd', alpha, Wh).reshape(n, H * D)
        return jax.nn.elu(out)

    def _L1_gnn_ref(inputs, adj, H_v):
        import jax, jax.numpy as jnp
        import numpy as np
        N = 8192
        D = 256
        DENSITY = 0.02
        scores = jnp.squeeze(inputs @ H_v, -1)
        mask = adj != 0.0
        logits = adj * scores[None, :]
        neg = jnp.asarray(jnp.finfo(logits.dtype).min, logits.dtype)
        logits = jnp.where(mask, logits, neg)
        m = jnp.max(logits, axis=1, keepdims=True)
        e = jnp.where(mask, jnp.exp(logits - m), 0.0)
        s = jnp.sum(e, axis=1, keepdims=True)
        weights = e / jnp.where(s > 0, s, 1.0)
        return weights @ inputs

    x = _layernorm(x + _L0_gnn_ref(x, adj, L0_gnn_W, L0_gnn_a), axis=-1)
    x = _layernorm(x + _L1_gnn_ref(x, adj, L1_gnn_H_v), axis=-1)
    return x


_drawn_inputs = setup_inputs


def setup_inputs(seed=0):
    import zlib

    import numpy as np

    out = dict(_drawn_inputs(seed))
    spreads = {}
    factors = {}
    for name, (base, spread) in spreads.items():
        noise = np.random.default_rng([zlib.crc32(name.encode()), seed]).standard_normal(out[name].shape)
        drawn = base * np.exp(spread * noise) if base else spread * noise
        out[name] = jnp.asarray(drawn.astype(out[name].dtype))
    for name, factor in factors.items():
        out[name] = (out[name] * factor).astype(out[name].dtype)
    return out
```

```python
import numpy as np
import concourse.bass as bass
from concourse import mybir
from contextlib import ExitStack

F32 = mybir.dt.float32
I32 = mybir.dt.int32
ALU = mybir.AluOpType
ACT = mybir.ActivationFunctionType
AX = mybir.AxisListType

P = 128
N = 8192
D = 256
H = 4
DH = D // H
T = N // P
HC = DH + 1
KC = D // P
EPS = 1e-5
SLOPE = 0.2
HIDDEN = -3.0e38
SEEN = -1.0e38


class Shared:

    def __init__(self, nc, ctx):
        def sb(name, shape, dt=F32):
            return ctx.enter_context(nc.sbuf_tensor(name, shape, dt))

        self.ident = sb("ident", [P, P])
        self.neg_half = sb("neg_half", [P, 1])
        self.wx = sb("wx", [P, KC, D + 2 * H])
        self.hv = sb("hv", [P, D])
        self.E = sb("E", [P, T, 2 * H])
        self.S = sb("S", [P, T])
        self.x1_dram = nc.dram_tensor("x1_dram", [N, D], F32, kind="Internal").ap()
        self.s_dram = nc.dram_tensor("s_dram", [1, N], F32, kind="Internal").ap()
        self.e_dram = nc.dram_tensor("e_dram", [H, N], F32, kind="Internal").ap()


def setup(nc, sh, W, a, hv):
    with ExitStack() as ctx:
        def sem(name):
            return ctx.enter_context(nc.semaphore(name))

        ab = ctx.enter_context(nc.sbuf_tensor("ab", [P, KC, 2 * H], F32))
        wt = ctx.enter_context(nc.sbuf_tensor("wt", [P, KC, D], F32))
        ps_t = ctx.enter_context(nc.psum_tensor("ps_wt", [P, KC, D], F32))
        ps_a = ctx.enter_context(nc.psum_tensor("ps_wa", [P, KC, 2 * H], F32))
        ab_zero, ident_zero, ident_made = sem("ab_zero"), sem("ident_zero"), sem("ident_made")
        w_loaded, a_loaded, hv_loaded = sem("w_loaded"), sem("a_loaded"), sem("hv_loaded")
        wt_made, wt_copied, wa_made, wa_copied = sem("wt_made"), sem("wt_copied"), sem("wa_made"), sem("wa_copied")
        block = ctx.enter_context(nc.Block())

        @block.sync
        def _(sp):
            for c in range(KC):
                sp.dma_start(sh.wx[:, c, 0:D], W[c * P:(c + 1) * P, :]).then_inc(w_loaded, 16)
            sp.dma_start(sh.hv[:, :], hv.rearrange("d o -> o d").to_broadcast([P, D])).then_inc(hv_loaded, 16)
            sp.wait_ge(ab_zero, 1)
            for h in range(H):
                c, p0 = h * DH // P, h * DH % P
                for side in range(2):
                    sp.dma_start(ab[p0:p0 + DH, c, side * H + h:side * H + h + 1],
                                 a[h:h + 1, side * DH:(side + 1) * DH].rearrange("o d -> d o")).then_inc(a_loaded, 16)
            sp.wait_ge(a_loaded, 16 * 2 * H)
            sp.wait_ge(w_loaded, 16 * KC)
            sp.wait_ge(hv_loaded, 16)

        @block.gpsimd
        def _(pool):
            pool.memset(ab[:, :, :], 0.0).then_inc(ab_zero, 1)
            pool.memset(sh.neg_half[:, :], -0.5)
            pool.memset(sh.ident[:, :], 0.0).then_inc(ident_zero, 1)
            pool.wait_ge(ident_zero, 1)
            pool.affine_select(out=sh.ident[:, :], in_=sh.ident[:, :], compare_op=ALU.not_equal, fill=1.0,
                               base=0, pattern=[[-1, P]], channel_multiplier=1).then_inc(ident_made, 1)

        @block.tensor
        def _(pe):
            pe.wait_ge(ident_made, 1)
            pe.wait_ge(w_loaded, 16 * KC)
            for c in range(KC):
                for b in range(KC):
                    last = pe.transpose(ps_t[:, b, c * P:(c + 1) * P], sh.wx[:, c, b * P:(b + 1) * P], sh.ident[:, :])
            last.then_inc(wt_made, 1)
            pe.wait_ge(wt_copied, 1)
            pe.wait_ge(a_loaded, 16 * 2 * H)
            for c in range(KC):
                for b in range(KC):
                    last = pe.matmul(ps_a[:, c, :], wt[:, b, c * P:(c + 1) * P], ab[:, b, :],
                                     start=(b == 0), stop=(b == KC - 1))
            last.then_inc(wa_made, 1)

        @block.vector
        def _(dve):
            dve.wait_ge(wt_made, 1)
            dve.tensor_copy(wt[:, :, :], ps_t[:, :, :]).then_inc(wt_copied, 1)
            dve.wait_ge(wa_made, 1)
            dve.tensor_copy(sh.wx[:, :, D:D + 2 * H], ps_a[:, :, :]).then_inc(wa_copied, 1)
            dve.wait_ge(wa_copied, 1)


def project(nc, sh, V, x):
    U = 8
    XB = 4
    with ExitStack() as ctx:
        def sem(name):
            return ctx.enter_context(nc.semaphore(name))

        X = ctx.enter_context(nc.sbuf_tensor("x_in", [P, 2, XB, D], F32))
        xt = ctx.enter_context(nc.sbuf_tensor("xt", [P, 2, D], F32))
        ps_x = [ctx.enter_context(nc.psum_tensor(f"ps_x{i}", [P, D], F32)) for i in range(2)]
        ps_w = [ctx.enter_context(nc.psum_tensor(f"ps_w{i}", [P, D + 2 * H], F32)) for i in range(2)]
        x_loaded = [sem(f"x_loaded{k}") for k in range(2)]
        x_used, xt_made = sem("x_used"), sem("xt_made")
        xt_copied, wh_made, wh_copied = sem("xt_copied"), sem("wh_made"), sem("wh_copied")
        block = ctx.enter_context(nc.Block())

        @block.sync
        def _(sp):
            with sp.Fori(0, T // U) as u:
                for k in range(2):
                    sp.wait_ge(x_used, u * 2 + (k + 1))
                    sp.dma_start(X[:, k, :, :],
                                 x[bass.ds((u * U + k * XB) * P, XB * P), :].rearrange("(t p) d -> p t d", p=P)
                                 ).then_inc(x_loaded[k], 16)
            for k in range(2):
                sp.wait_ge(x_loaded[k], 16 * T // U)

        @block.tensor
        def _(pe):
            pe.sem_inc(x_used, 2)

            def transpose_x(u, b):
                if b % XB == 0:
                    pe.wait_ge(x_loaded[b // XB], u * 16 + 16)
                pe.wait_ge(xt_copied, u * U + (b + 1))
                for c in range(KC):
                    last = pe.transpose(ps_x[b % 2][:, c * P:(c + 1) * P],
                                        X[:, b // XB, b % XB, c * P:(c + 1) * P], sh.ident[:, :])
                last.then_inc(xt_made, 1)
                if b % XB == XB - 1:
                    pe.drain().then_inc(x_used, 1)

            with pe.Fori(0, T // U) as u:
                transpose_x(u, 0)
                for b in range(U):
                    if b + 1 < U:
                        transpose_x(u, b + 1)
                    pe.wait_ge(xt_copied, u * U + (b + 3))
                    pe.wait_ge(wh_copied, u * U + (b + 1))
                    for c in range(KC):
                        last = pe.matmul(ps_w[b % 2][:, :], xt[:, b % 2, c * P:(c + 1) * P], sh.wx[:, c, :],
                                         start=(c == 0), stop=(c == KC - 1))
                    last.then_inc(wh_made, 1)

        @block.vector
        def _(dve):
            dve.sem_inc(xt_copied, 2)
            with dve.Fori(0, T // U) as u:
                for b in range(U):
                    dve.wait_ge(xt_made, u * U + (b + 1))
                    dve.tensor_copy(xt[:, b % 2, :], ps_x[b % 2][:, :]).then_inc(xt_copied, 1)

        @block.scalar
        def _(act):
            act.sem_inc(wh_copied, 2)
            with act.Fori(0, T // U) as u:
                for b in range(U):
                    act.wait_ge(wh_made, u * U + (b + 1))
                    act.activation(V[:, bass.ds(u * U + b, 1), :, 0:DH].squeeze(1),
                                   ps_w[b % 2][:, 0:D].rearrange("p (h d) -> p h d", h=H), ACT.Copy)
                    act.activation(sh.E[:, bass.ds(u * U + b, 1), :].squeeze(1),
                                   ps_w[b % 2][:, D:D + 2 * H], ACT.Copy).then_inc(wh_copied, 1)


GB = 4
NG = T // GB


def attend_pe(pe, sh, z, pt, ps_t, acc, n, rhs, z_made, zt_made, pt_copied, pt_used, acc_free, acc_made):
    def transpose_group(g):
        pe.wait_ge(pt_copied, n * NG + (g + 1))
        for b in range(GB):
            j = g * GB + b
            last = pe.transpose(ps_t[g % 2][:, b * P:(b + 1) * P], z[:, j * P:(j + 1) * P], sh.ident[:, :])
        last.then_inc(zt_made, 1)

    pe.wait_ge(z_made, n + 1)
    pe.wait_ge(acc_free, n + 1)
    transpose_group(0)
    for g in range(NG):
        if g + 1 < NG:
            transpose_group(g + 1)
        pe.wait_ge(pt_copied, n * NG + (g + 3))
        for b in range(GB):
            j = g * GB + b
            last = pe.matmul(acc, pt[:, g % 2, b * P:(b + 1) * P], rhs(j), start=(j == 0), stop=(j == T - 1))
        last.then_inc(pt_used, 1)
    pe.drain().then_inc(acc_made, 1)


def attend_act(act, z, neg_max, pt, ps_t, n, z_ready, z_made, zt_made, pt_copied, pt_used):
    act.wait_ge(z_ready, n + 1)
    act.activation(z[:, :], z[:, :], ACT.Exp, bias=neg_max[:, 0:1], scale=1.0).then_inc(z_made, 1)
    for g in range(NG):
        act.wait_ge(zt_made, n * NG + (g + 1))
        act.wait_ge(pt_used, n * NG + (g + 1))
        act.activation(pt[:, g % 2, :], ps_t[g % 2][:, :], ACT.Copy).then_inc(pt_copied, 1)


def layernorm_dve(dve, y, out, st, mv, var_made, rstd_made, count):
    dve.drain()
    dve.bn_stats(st[:, :], y[:, :])
    dve.drain()
    dve.bn_aggr(mv[:, :], st[:, :])
    dve.drain()
    dve.tensor_scalar_add(mv[:, 1:2], mv[:, 1:2], EPS).then_inc(var_made, 1)
    dve.wait_ge(rstd_made, count)
    return dve.tensor_scalar(out[:, :], y[:, :], mv[:, 0:1], mv[:, 1:2], ALU.subtract, ALU.mult)


def rstd_pool(pool, sh, mv, var_made, rstd_made, count):
    pool.wait_ge(var_made, count)
    pool.tensor_tensor(out=mv[:, 1:2], in0=mv[:, 1:2], in1=sh.neg_half[:, :], op=ALU.pow).then_inc(rstd_made, 1)


def general_layer0(nc, sh, V, x, adj):
    with ExitStack() as ctx:
        def sem(name):
            return ctx.enter_context(nc.semaphore(name))

        def sb(name, shape, dt=F32):
            return ctx.enter_context(nc.sbuf_tensor(name, shape, dt))

        A = sb("g0_adj", [P, N])
        z = sb("g0_z", [P, N])
        eb = sb("g0_eb", [P, N])
        xin, agg, ex, y, out1 = (sb(f"g0_{s}", [P, D]) for s in ("x", "agg", "ex", "y", "out"))
        pt = sb("g0_pt", [P, 2, GB * P])
        neg_max, m, own, r = (sb(f"g0_{s}", [P, 1]) for s in ("nm", "m", "own", "r"))
        st, mv, s1 = sb("g0_st", [P, 6]), sb("g0_mv", [P, 2]), sb("g0_s1", [P, 1])
        ps_t = [ctx.enter_context(nc.psum_tensor(f"g0_pst{i}", [P, GB * P], F32)) for i in range(2)]
        acc = ctx.enter_context(nc.psum_tensor("g0_acc", [P, HC], F32))
        e_stored, e_ready = sem("e_stored"), sem("e_ready")
        adj_loaded, x_loaded, eb_loaded = sem("g0_adj_loaded"), sem("g0_x_loaded"), sem("g0_eb_loaded")
        tile_done, eb_used = sem("g0_tile_done"), sem("g0_eb_used")
        z_ready, z_made, zt_made, pt_copied = sem("g0_z_ready"), sem("g0_z_made"), sem("g0_zt_made"), sem("g0_pt_copied")
        pt_used, acc_free, acc_made = sem("g0_pt_used"), sem("g0_acc_free"), sem("g0_acc_made")
        low_made, ex_made, var_made, rstd_made = sem("g0_low"), sem("g0_ex"), sem("g0_var"), sem("g0_rstd")
        x1_made, x1_stored, s_made, s_stored = sem("g0_x1_made"), sem("g0_x1_stored"), sem("g0_s_made"), sem("g0_s_stored")
        block = ctx.enter_context(nc.Block())

        @block.sync
        def _(sp):
            with nc.allow_non_contiguous_dma("e_j as rows, once"):
                for h in range(H):
                    sp.dma_start(sh.e_dram[h, :].rearrange("(t p) -> p t", p=P), sh.E[:, :, H + h]).then_inc(e_stored, 16)
            sp.wait_ge(e_stored, 16 * H)
            with sp.Fori(0, T) as t:
                sp.wait_ge(tile_done, t + 1)
                sp.dma_start(A[:, :], adj[bass.ds(t * P, P), :]).then_inc(adj_loaded, 16)
                sp.dma_start(xin[:, :], x[bass.ds(t * P, P), :]).then_inc(x_loaded, 16)
                for h in range(H):
                    sp.wait_ge(eb_used, t * H + (h + 1))
                    sp.dma_start(eb[:, :], sh.e_dram[h:h + 1, :].to_broadcast([P, N])).then_inc(eb_loaded, 16)
                sp.wait_ge(x1_made, t + 1)
                sp.dma_start(sh.x1_dram[bass.ds(t * P, P), :], out1[:, :]).then_inc(x1_stored, 16)
            sp.wait_ge(x1_stored, 16 * T)
            sp.wait_ge(s_made, T)
            with nc.allow_non_contiguous_dma("the scores as a row, once"):
                sp.dma_start(sh.s_dram[0, :].rearrange("(t p) -> p t", p=P), sh.S[:, :]).then_inc(s_stored, 16)
            sp.wait_ge(s_stored, 16)

        @block.vector
        def _(dve):
            dve.sem_inc(tile_done, 1)
            dve.sem_inc(eb_used, 1)
            dve.sem_inc(acc_free, 1)
            with dve.Fori(0, T) as t:
                dve.wait_ge(adj_loaded, t * 16 + 16)
                dve.tensor_scalar(z[:, :], A[:, :], 0.0, HIDDEN, ALU.is_equal, ALU.mult)
                dve.drain()
                dve.tensor_tensor(out=A[:, :], in0=A[:, :], in1=z[:, :], op=ALU.add)
                dve.drain()
                for h in range(H):
                    dve.wait_ge(eb_loaded, (t * H + h) * 16 + 16)
                    dve.tensor_scalar(z[:, :], eb[:, :], sh.E[:, bass.ds(t, 1), h:h + 1].squeeze(1), None, ALU.add).then_inc(eb_used, 1)
                    dve.drain()
                    dve.scalar_tensor_tensor(out=z[:, :], in0=z[:, :], scalar=SLOPE, in1=z[:, :],
                                             op0=ALU.mult, op1=ALU.max)
                    dve.drain()
                    dve.tensor_tensor(out=z[:, :], in0=z[:, :], in1=A[:, :], op=ALU.add)
                    dve.drain()
                    dve.reduce_max(m[:, :], z[:, :], AX.X)
                    dve.drain()
                    dve.tensor_scalar(own[:, :], m[:, :], SEEN, None, ALU.is_lt)
                    dve.tensor_scalar(neg_max[:, :], m[:, :], -1.0, None, ALU.mult).then_inc(z_ready, 1)
                    dve.wait_ge(acc_made, (t * H + h) + 1)
                    dve.reciprocal(r[:, :], acc[:, DH:HC])
                    dve.tensor_scalar(y[:, 0:DH], V[:, bass.ds(t, 1), h, 0:DH].squeeze(1), own[:, 0:1], None, ALU.mult)
                    dve.tensor_scalar(own[:, :], own[:, :], -1.0, 1.0, ALU.mult, ALU.add)
                    dve.drain()
                    dve.tensor_tensor(out=r[:, :], in0=r[:, :], in1=own[:, :], op=ALU.mult)
                    dve.drain()
                    dve.scalar_tensor_tensor(out=agg[:, h * DH:(h + 1) * DH], in0=acc[:, 0:DH], scalar=r[:, 0:1],
                                             in1=y[:, 0:DH], op0=ALU.mult, op1=ALU.add).then_inc(acc_free, 1)
                    dve.drain()
                dve.tensor_scalar(ex[:, :], agg[:, :], 0.0, None, ALU.min).then_inc(low_made, 1)
                dve.wait_ge(ex_made, t + 1)
                dve.scalar_tensor_tensor(out=y[:, :], in0=agg[:, :], scalar=0.0, in1=ex[:, :], op0=ALU.max, op1=ALU.add)
                dve.drain()
                dve.wait_ge(x_loaded, t * 16 + 16)
                dve.scalar_tensor_tensor(out=y[:, :], in0=y[:, :], scalar=-1.0, in1=xin[:, :], op0=ALU.add, op1=ALU.add).then_inc(tile_done, 1)
                layernorm_dve(dve, y, out1, st, mv, var_made, rstd_made, t + 1)
                dve.drain()
                dve.tensor_tensor_reduce(out=ex[:, :], in0=out1[:, :], in1=sh.hv[:, :], scale=1.0, scalar=0.0,
                                         op0=ALU.mult, op1=ALU.add, accum_out=s1[:, 0:1])
                dve.drain()
                dve.tensor_copy(sh.S[:, bass.ds(t, 1)], s1[:, :]).then_inc(s_made, 1)
                dve.drain().then_inc(x1_made, 1)
                dve.wait_ge(x1_stored, t * 16 + 16)

        @block.gpsimd
        def _(pool):
            with pool.Fori(0, T) as t:
                rstd_pool(pool, sh, mv, var_made, rstd_made, t + 1)

        @block.scalar
        def _(act):
            act.sem_inc(pt_copied, 2)
            with act.Fori(0, T) as t:
                for h in range(H):
                    attend_act(act, z, neg_max, pt, ps_t, t * H + h, z_ready, z_made, zt_made, pt_copied, pt_used)
                act.wait_ge(low_made, t + 1)
                act.activation(ex[:, :], ex[:, :], ACT.Exp).then_inc(ex_made, 1)

        @block.tensor
        def _(pe):
            pe.sem_inc(pt_used, 2)
            with pe.Fori(0, T) as t:
                for h in range(H):
                    attend_pe(pe, sh, z, pt, ps_t, acc[:, :], t * H + h, lambda j: V[:, j, h, :],
                              z_made, zt_made, pt_copied, pt_used, acc_free, acc_made)


def general_layer1(nc, sh, adj, out):
    CH = 2048
    with ExitStack() as ctx:
        def sem(name):
            return ctx.enter_context(nc.semaphore(name))

        def sb(name, shape, dt=F32):
            return ctx.enter_context(nc.sbuf_tensor(name, shape, dt))

        X1 = sb("g1_x1", [P, T, D + 1])
        A = sb("g1_adj", [P, N])
        z = sb("g1_z", [P, N])
        sbc = sb("g1_s", [P, N])
        hide = sb("g1_hide", [P, CH])
        y, out1 = sb("g1_y", [P, D]), sb("g1_out", [P, D])
        pt = sb("g1_pt", [P, 2, GB * P])
        neg_max, m, seen, r = (sb(f"g1_{s}", [P, 1]) for s in ("nm", "m", "seen", "r"))
        st, mv = sb("g1_st", [P, 6]), sb("g1_mv", [P, 2])
        ps_t = [ctx.enter_context(nc.psum_tensor(f"g1_pst{i}", [P, GB * P], F32)) for i in range(2)]
        acc = ctx.enter_context(nc.psum_tensor("g1_acc", [P, D + 1], F32))
        x1_loaded, s_loaded, adj_loaded, adj_used = sem("g1_x1"), sem("g1_s_loaded"), sem("g1_adj_loaded"), sem("g1_adj_used")
        ones_made = sem("g1_ones")
        z_ready, z_made, zt_made, pt_copied = sem("g1_z_ready"), sem("g1_z_made"), sem("g1_zt_made"), sem("g1_pt_copied")
        pt_used, acc_free, acc_made = sem("g1_pt_used"), sem("g1_acc_free"), sem("g1_acc_made")
        var_made, rstd_made, y_made, y_stored = sem("g1_var"), sem("g1_rstd"), sem("g1_y_made"), sem("g1_y_stored")
        block = ctx.enter_context(nc.Block())

        @block.sync
        def _(sp):
            sp.dma_start(X1[:, :, 0:D], sh.x1_dram.rearrange("(t p) d -> p t d", p=P)).then_inc(x1_loaded, 16)
            sp.dma_start(sbc[:, :], sh.s_dram[0:1, :].to_broadcast([P, N])).then_inc(s_loaded, 16)
            with sp.Fori(0, T) as t:
                sp.wait_ge(adj_used, t + 1)
                sp.dma_start(A[:, :], adj[bass.ds(t * P, P), :]).then_inc(adj_loaded, 16)
                sp.wait_ge(y_made, t + 1)
                sp.dma_start(out[bass.ds(t * P, P), :], out1[:, :]).then_inc(y_stored, 16)
            sp.wait_ge(y_stored, 16 * T)

        @block.vector
        def _(dve):
            dve.sem_inc(adj_used, 1)
            dve.sem_inc(acc_free, 1)
            dve.wait_ge(s_loaded, 16)
            dve.wait_ge(x1_loaded, 16)
            with dve.Fori(0, T) as t:
                dve.wait_ge(adj_loaded, t * 16 + 16)
                dve.tensor_tensor(out=z[:, :], in0=A[:, :], in1=sbc[:, :], op=ALU.mult)
                for c in range(N // CH):
                    cs = slice(c * CH, (c + 1) * CH)
                    dve.drain()
                    dve.tensor_scalar(hide[:, :], A[:, cs], 0.0, HIDDEN, ALU.is_equal, ALU.mult)
                    dve.drain()
                    dve.tensor_tensor(out=z[:, cs], in0=z[:, cs], in1=hide[:, :], op=ALU.add)
                dve.drain().then_inc(adj_used, 1)
                dve.reduce_max(m[:, :], z[:, :], AX.X)
                dve.drain()
                dve.tensor_scalar(seen[:, :], m[:, :], SEEN, None, ALU.is_ge)
                dve.tensor_scalar(neg_max[:, :], m[:, :], -1.0, None, ALU.mult).then_inc(z_ready, 1)
                dve.wait_ge(acc_made, t + 1)
                dve.reciprocal(r[:, :], acc[:, D:D + 1])
                dve.drain()
                dve.tensor_tensor(out=r[:, :], in0=r[:, :], in1=seen[:, :], op=ALU.mult)
                dve.drain()
                dve.scalar_tensor_tensor(out=y[:, :], in0=acc[:, 0:D], scalar=r[:, 0:1],
                                         in1=X1[:, bass.ds(t, 1), 0:D].squeeze(1), op0=ALU.mult, op1=ALU.add).then_inc(acc_free, 1)
                layernorm_dve(dve, y, out1, st, mv, var_made, rstd_made, t + 1).then_inc(y_made, 1)
                dve.wait_ge(y_stored, t * 16 + 16)

        @block.gpsimd
        def _(pool):
            pool.memset(X1[:, :, D:D + 1], 1.0).then_inc(ones_made, 1)
            with pool.Fori(0, T) as t:
                rstd_pool(pool, sh, mv, var_made, rstd_made, t + 1)

        @block.scalar
        def _(act):
            act.sem_inc(pt_copied, 2)
            with act.Fori(0, T) as t:
                attend_act(act, z, neg_max, pt, ps_t, t, z_ready, z_made, zt_made, pt_copied, pt_used)

        @block.tensor
        def _(pe):
            pe.sem_inc(pt_used, 2)
            pe.wait_ge(ones_made, 1)
            pe.wait_ge(x1_loaded, 16)
            with pe.Fori(0, T) as t:
                attend_pe(pe, sh, z, pt, ps_t, acc[:, :], t, lambda j: X1[:, j, :],
                          z_made, zt_made, pt_copied, pt_used, acc_free, acc_made)


def general(nc, sh, x, adj, out):
    with nc.sbuf_tensor("V_general", [P, T, H, HC], F32) as V:
        with nc.semaphore("ones_in_v") as ones_in_v, nc.Block() as block:
            @block.gpsimd
            def _(pool):
                pool.memset(V[:, :, :, DH:HC], 1.0).then_inc(ones_in_v, 1)
                pool.wait_ge(ones_in_v, 1)
        project(nc, sh, V, x)
        general_layer0(nc, sh, V, x, adj)
    general_layer1(nc, sh, adj, out)


def program(nc, x, adj, W, a, hv, out):
    with ExitStack() as ctx:
        sh = Shared(nc, ctx)
        setup(nc, sh, W, a, hv)
        general(nc, sh, x, adj, out)


_INS = ['x', 'adj', 'L0_gnn_W', 'L0_gnn_a', 'L1_gnn_H_v']
_OUTS = [((N, D), 'float32')]


def kernel(**inputs):
    import numpy as _np
    import concourse.bacc as _bacc
    from concourse import mybir as _mybir
    from concourse.bass_utils import run_bass_kernel_spmd as _run

    nc = _bacc.Bacc("TRN2", target_bir_lowering=False, num_devices=1)
    arrays, args = {}, []
    for name in _INS:
        a = _np.ascontiguousarray(inputs[name])
        arrays[f"in_{name}_dram"] = a
        args.append(nc.dram_tensor(f"in_{name}_dram", a.shape, _mybir.dt.from_np(a.dtype), kind="ExternalInput").ap())
    for i, (shape, dtype) in enumerate(_OUTS):
        dt = _mybir.dt.from_np(_np.dtype(dtype))
        args.append(nc.dram_tensor(f"out_{i}_dram", shape, dt, kind="ExternalOutput").ap())
    program(nc, *args)
    r = _run(nc, [arrays], core_ids=[0])
    return r.results[0]["out_0_dram"]
```

```python
import numpy as np
import concourse.bass as bass
from concourse import mybir
from contextlib import ExitStack

F32 = mybir.dt.float32
I32 = mybir.dt.int32
ALU = mybir.AluOpType
ACT = mybir.ActivationFunctionType
AX = mybir.AxisListType

P = 128
N = 8192
D = 256
H = 4
DH = D // H
T = N // P
HC = DH + 1
KC = D // P
EPS = 1e-5
SLOPE = 0.2
HIDDEN = -3.0e38
SEEN = -1.0e38


class Shared:

    def __init__(self, nc, ctx):
        def sb(name, shape, dt=F32):
            return ctx.enter_context(nc.sbuf_tensor(name, shape, dt))

        self.ident = sb("ident", [P, P])
        self.neg_half = sb("neg_half", [P, 1])
        self.wx = sb("wx", [P, KC, D + 2 * H])
        self.hv = sb("hv", [P, D])
        self.E = sb("E", [P, T, 2 * H])
        self.S = sb("S", [P, T])
        self.x1_dram = nc.dram_tensor("x1_dram", [N, D], F32, kind="Internal").ap()
        self.s_dram = nc.dram_tensor("s_dram", [1, N], F32, kind="Internal").ap()
        self.e_dram = nc.dram_tensor("e_dram", [H, N], F32, kind="Internal").ap()
        self.a_dram = nc.dram_tensor("a_dram", [H, N], F32, kind="Internal").ap()


def setup(nc, sh, W, a, hv):
    with ExitStack() as ctx:
        def sem(name):
            return ctx.enter_context(nc.semaphore(name))

        ab = ctx.enter_context(nc.sbuf_tensor("ab", [P, KC, 2 * H], F32))
        wt = ctx.enter_context(nc.sbuf_tensor("wt", [P, KC, D], F32))
        ps_t = ctx.enter_context(nc.psum_tensor("ps_wt", [P, KC, D], F32))
        ps_a = ctx.enter_context(nc.psum_tensor("ps_wa", [P, KC, 2 * H], F32))
        ab_zero, ident_zero, ident_made = sem("ab_zero"), sem("ident_zero"), sem("ident_made")
        w_loaded, a_loaded, hv_loaded = sem("w_loaded"), sem("a_loaded"), sem("hv_loaded")
        wt_made, wt_copied, wa_made, wa_copied = sem("wt_made"), sem("wt_copied"), sem("wa_made"), sem("wa_copied")
        block = ctx.enter_context(nc.Block())

        @block.sync
        def _(sp):
            for c in range(KC):
                sp.dma_start(sh.wx[:, c, 0:D], W[c * P:(c + 1) * P, :]).then_inc(w_loaded, 16)
            sp.dma_start(sh.hv[:, :], hv.rearrange("d o -> o d").to_broadcast([P, D])).then_inc(hv_loaded, 16)
            sp.wait_ge(ab_zero, 1)
            for h in range(H):
                c, p0 = h * DH // P, h * DH % P
                for side in range(2):
                    sp.dma_start(ab[p0:p0 + DH, c, side * H + h:side * H + h + 1],
                                 a[h:h + 1, side * DH:(side + 1) * DH].rearrange("o d -> d o")).then_inc(a_loaded, 16)
            sp.wait_ge(a_loaded, 16 * 2 * H)
            sp.wait_ge(w_loaded, 16 * KC)
            sp.wait_ge(hv_loaded, 16)

        @block.gpsimd
        def _(pool):
            pool.memset(ab[:, :, :], 0.0).then_inc(ab_zero, 1)
            pool.memset(sh.neg_half[:, :], -0.5)
            pool.memset(sh.ident[:, :], 0.0).then_inc(ident_zero, 1)
            pool.wait_ge(ident_zero, 1)
            pool.affine_select(out=sh.ident[:, :], in_=sh.ident[:, :], compare_op=ALU.not_equal, fill=1.0,
                               base=0, pattern=[[-1, P]], channel_multiplier=1).then_inc(ident_made, 1)

        @block.tensor
        def _(pe):
            pe.wait_ge(ident_made, 1)
            pe.wait_ge(w_loaded, 16 * KC)
            for c in range(KC):
                for b in range(KC):
                    last = pe.transpose(ps_t[:, b, c * P:(c + 1) * P], sh.wx[:, c, b * P:(b + 1) * P], sh.ident[:, :])
            last.then_inc(wt_made, 1)
            pe.wait_ge(wt_copied, 1)
            pe.wait_ge(a_loaded, 16 * 2 * H)
            for c in range(KC):
                for b in range(KC):
                    last = pe.matmul(ps_a[:, c, :], wt[:, b, c * P:(c + 1) * P], ab[:, b, :],
                                     start=(b == 0), stop=(b == KC - 1))
            last.then_inc(wa_made, 1)

        @block.vector
        def _(dve):
            dve.wait_ge(wt_made, 1)
            dve.tensor_copy(wt[:, :, :], ps_t[:, :, :]).then_inc(wt_copied, 1)
            dve.wait_ge(wa_made, 1)
            dve.tensor_copy(sh.wx[:, :, D:D + 2 * H], ps_a[:, :, :]).then_inc(wa_copied, 1)
            dve.wait_ge(wa_copied, 1)


def project(nc, sh, V, x, path, adj=None, first_max=None):
    U = 8
    XB = 4
    with ExitStack() as ctx:
        def sem(name):
            return ctx.enter_context(nc.semaphore(path + name))

        X = ctx.enter_context(nc.sbuf_tensor(path + "x_in", [P, 2, XB, D], F32))
        xt = ctx.enter_context(nc.sbuf_tensor(path + "xt", [P, 2, D], F32))
        if adj is not None:
            QX = N * U // T
            first = ctx.enter_context(nc.sbuf_tensor(path + "first", [P, IT, QX], F32))
            part = ctx.enter_context(nc.sbuf_tensor(path + "part", [P, IT], F32))
            first_loaded = [sem(f"first_loaded{it}") for it in range(IT)]
            first_read = sem("first_read")
        ps_x = [ctx.enter_context(nc.psum_tensor(f"{path}ps_x{i}", [P, D], F32)) for i in range(2)]
        ps_w = [ctx.enter_context(nc.psum_tensor(f"{path}ps_w{i}", [P, D + 2 * H], F32)) for i in range(2)]
        x_loaded = [sem(f"x_loaded{k}") for k in range(2)]
        x_used, xt_made = sem("x_used"), sem("xt_made")
        xt_copied, wh_made, wh_copied = sem("xt_copied"), sem("wh_made"), sem("wh_copied")
        block = ctx.enter_context(nc.Block())

        @block.sync
        def _(sp):
            def load_first(u, it):
                sp.wait_ge(first_read, u * IT + (it + 1))
                sp.dma_start(first[:, it, :], adj[it * P:(it + 1) * P, bass.ds(u * QX, QX)]).then_inc(first_loaded[it], 16)

            with sp.Fori(0, T // U) as u:
                for k in range(2):
                    if adj is not None:
                        load_first(u, 2 * k)
                    sp.wait_ge(x_used, u * 2 + (k + 1))
                    sp.dma_start(X[:, k, :, :],
                                 x[bass.ds((u * U + k * XB) * P, XB * P), :].rearrange("(t p) d -> p t d", p=P)
                                 ).then_inc(x_loaded[k], 16)
                    if adj is not None:
                        load_first(u, 2 * k + 1)
            for k in range(2):
                sp.wait_ge(x_loaded[k], 16 * T // U)

        @block.tensor
        def _(pe):
            pe.sem_inc(x_used, 2)

            def transpose_x(u, b):
                if b % XB == 0:
                    pe.wait_ge(x_loaded[b // XB], u * 16 + 16)
                pe.wait_ge(xt_copied, u * U + (b + 1))
                for c in range(KC):
                    last = pe.transpose(ps_x[b % 2][:, c * P:(c + 1) * P],
                                        X[:, b // XB, b % XB, c * P:(c + 1) * P], sh.ident[:, :])
                last.then_inc(xt_made, 1)
                if b % XB == XB - 1:
                    pe.drain().then_inc(x_used, 1)

            with pe.Fori(0, T // U) as u:
                transpose_x(u, 0)
                for b in range(U):
                    if b + 1 < U:
                        transpose_x(u, b + 1)
                    pe.wait_ge(xt_copied, u * U + (b + 3))
                    pe.wait_ge(wh_copied, u * U + (b + 1))
                    for c in range(KC):
                        last = pe.matmul(ps_w[b % 2][:, :], xt[:, b % 2, c * P:(c + 1) * P], sh.wx[:, c, :],
                                         start=(c == 0), stop=(c == KC - 1))
                    last.then_inc(wh_made, 1)

        @block.vector
        def _(dve):
            dve.sem_inc(xt_copied, 2)
            if adj is not None:
                dve.sem_inc(first_read, IT)
            with dve.Fori(0, T // U) as u:
                for b in range(U):
                    dve.wait_ge(xt_made, u * U + (b + 1))
                    dve.tensor_copy(xt[:, b % 2, :], ps_x[b % 2][:, :]).then_inc(xt_copied, 1)
                    if adj is not None and b % 2 == 1:
                        it = b // 2
                        dve.wait_ge(first_loaded[it], u * 16 + 16)
                        dve.reduce_max(part[:, it:it + 1], first[:, it, :], AX.X).then_inc(first_read, 1)
                if adj is not None:
                    dve.drain()
                    dve.tensor_copy(first_max[:, bass.ds(u, 1), :].squeeze(1), part[:, :])
                    dve.drain()

        @block.scalar
        def _(act):
            act.sem_inc(wh_copied, 2)
            with act.Fori(0, T // U) as u:
                for b in range(U):
                    act.wait_ge(wh_made, u * U + (b + 1))
                    act.activation(V[:, bass.ds(u * U + b, 1), :, 0:DH].squeeze(1),
                                   ps_w[b % 2][:, 0:D].rearrange("p (h d) -> p h d", h=H), ACT.Copy)
                    act.activation(sh.E[:, bass.ds(u * U + b, 1), :].squeeze(1),
                                   ps_w[b % 2][:, D:D + 2 * H], ACT.Copy).then_inc(wh_copied, 1)


GB = 4
NG = T // GB


def attend_pe(pe, sh, z, pt, ps_t, acc, n, rhs, z_made, zt_made, pt_copied, pt_used, acc_free, acc_made):
    def transpose_group(g):
        pe.wait_ge(pt_copied, n * NG + (g + 1))
        for b in range(GB):
            j = g * GB + b
            last = pe.transpose(ps_t[g % 2][:, b * P:(b + 1) * P], z[:, j * P:(j + 1) * P], sh.ident[:, :])
        last.then_inc(zt_made, 1)

    pe.wait_ge(z_made, n + 1)
    pe.wait_ge(acc_free, n + 1)
    transpose_group(0)
    for g in range(NG):
        if g + 1 < NG:
            transpose_group(g + 1)
        pe.wait_ge(pt_copied, n * NG + (g + 3))
        for b in range(GB):
            j = g * GB + b
            last = pe.matmul(acc, pt[:, g % 2, b * P:(b + 1) * P], rhs(j), start=(j == 0), stop=(j == T - 1))
        last.then_inc(pt_used, 1)
    pe.drain().then_inc(acc_made, 1)


def attend_act(act, z, neg_max, pt, ps_t, n, z_ready, z_made, zt_made, pt_copied, pt_used):
    act.wait_ge(z_ready, n + 1)
    act.activation(z[:, :], z[:, :], ACT.Exp, bias=neg_max[:, 0:1], scale=1.0).then_inc(z_made, 1)
    for g in range(NG):
        act.wait_ge(zt_made, n * NG + (g + 1))
        act.wait_ge(pt_used, n * NG + (g + 1))
        act.activation(pt[:, g % 2, :], ps_t[g % 2][:, :], ACT.Copy).then_inc(pt_copied, 1)


def layernorm_dve(dve, y, out, st, mv, var_made, rstd_made, count):
    dve.drain()
    dve.bn_stats(st[:, :], y[:, :])
    dve.drain()
    dve.bn_aggr(mv[:, :], st[:, :])
    dve.drain()
    dve.tensor_scalar_add(mv[:, 1:2], mv[:, 1:2], EPS).then_inc(var_made, 1)
    dve.wait_ge(rstd_made, count)
    return dve.tensor_scalar(out[:, :], y[:, :], mv[:, 0:1], mv[:, 1:2], ALU.subtract, ALU.mult)


def rstd_pool(pool, sh, mv, var_made, rstd_made, count):
    pool.wait_ge(var_made, count)
    pool.tensor_tensor(out=mv[:, 1:2], in0=mv[:, 1:2], in1=sh.neg_half[:, :], op=ALU.pow).then_inc(rstd_made, 1)


def general_layer0(nc, sh, V, x, adj):
    with ExitStack() as ctx:
        def sem(name):
            return ctx.enter_context(nc.semaphore(name))

        def sb(name, shape, dt=F32):
            return ctx.enter_context(nc.sbuf_tensor(name, shape, dt))

        A = sb("g0_adj", [P, N])
        z = sb("g0_z", [P, N])
        eb = sb("g0_eb", [P, N])
        xin, agg, ex, y, out1 = (sb(f"g0_{s}", [P, D]) for s in ("x", "agg", "ex", "y", "out"))
        pt = sb("g0_pt", [P, 2, GB * P])
        neg_max, m, own, r = (sb(f"g0_{s}", [P, 1]) for s in ("nm", "m", "own", "r"))
        st, mv, s1 = sb("g0_st", [P, 6]), sb("g0_mv", [P, 2]), sb("g0_s1", [P, 1])
        ps_t = [ctx.enter_context(nc.psum_tensor(f"g0_pst{i}", [P, GB * P], F32)) for i in range(2)]
        acc = ctx.enter_context(nc.psum_tensor("g0_acc", [P, HC], F32))
        e_stored, e_ready = sem("e_stored"), sem("e_ready")
        adj_loaded, x_loaded, eb_loaded = sem("g0_adj_loaded"), sem("g0_x_loaded"), sem("g0_eb_loaded")
        tile_done, eb_used = sem("g0_tile_done"), sem("g0_eb_used")
        z_ready, z_made, zt_made, pt_copied = sem("g0_z_ready"), sem("g0_z_made"), sem("g0_zt_made"), sem("g0_pt_copied")
        pt_used, acc_free, acc_made = sem("g0_pt_used"), sem("g0_acc_free"), sem("g0_acc_made")
        low_made, ex_made, var_made, rstd_made = sem("g0_low"), sem("g0_ex"), sem("g0_var"), sem("g0_rstd")
        x1_made, x1_stored, s_made, s_stored = sem("g0_x1_made"), sem("g0_x1_stored"), sem("g0_s_made"), sem("g0_s_stored")
        block = ctx.enter_context(nc.Block())

        @block.sync
        def _(sp):
            with nc.allow_non_contiguous_dma("e_j as rows, once"):
                for h in range(H):
                    sp.dma_start(sh.e_dram[h, :].rearrange("(t p) -> p t", p=P), sh.E[:, :, H + h]).then_inc(e_stored, 16)
            sp.wait_ge(e_stored, 16 * H)
            with sp.Fori(0, T) as t:
                sp.wait_ge(tile_done, t + 1)
                sp.dma_start(A[:, :], adj[bass.ds(t * P, P), :]).then_inc(adj_loaded, 16)
                sp.dma_start(xin[:, :], x[bass.ds(t * P, P), :]).then_inc(x_loaded, 16)
                for h in range(H):
                    sp.wait_ge(eb_used, t * H + (h + 1))
                    sp.dma_start(eb[:, :], sh.e_dram[h:h + 1, :].to_broadcast([P, N])).then_inc(eb_loaded, 16)
                sp.wait_ge(x1_made, t + 1)
                sp.dma_start(sh.x1_dram[bass.ds(t * P, P), :], out1[:, :]).then_inc(x1_stored, 16)
            sp.wait_ge(x1_stored, 16 * T)
            sp.wait_ge(s_made, T)
            with nc.allow_non_contiguous_dma("the scores as a row, once"):
                sp.dma_start(sh.s_dram[0, :].rearrange("(t p) -> p t", p=P), sh.S[:, :]).then_inc(s_stored, 16)
            sp.wait_ge(s_stored, 16)

        @block.vector
        def _(dve):
            dve.sem_inc(tile_done, 1)
            dve.sem_inc(eb_used, 1)
            dve.sem_inc(acc_free, 1)
            with dve.Fori(0, T) as t:
                dve.wait_ge(adj_loaded, t * 16 + 16)
                dve.tensor_scalar(z[:, :], A[:, :], 0.0, HIDDEN, ALU.is_equal, ALU.mult)
                dve.drain()
                dve.tensor_tensor(out=A[:, :], in0=A[:, :], in1=z[:, :], op=ALU.add)
                dve.drain()
                for h in range(H):
                    dve.wait_ge(eb_loaded, (t * H + h) * 16 + 16)
                    dve.tensor_scalar(z[:, :], eb[:, :], sh.E[:, bass.ds(t, 1), h:h + 1].squeeze(1), None, ALU.add).then_inc(eb_used, 1)
                    dve.drain()
                    dve.scalar_tensor_tensor(out=z[:, :], in0=z[:, :], scalar=SLOPE, in1=z[:, :],
                                             op0=ALU.mult, op1=ALU.max)
                    dve.drain()
                    dve.tensor_tensor(out=z[:, :], in0=z[:, :], in1=A[:, :], op=ALU.add)
                    dve.drain()
                    dve.reduce_max(m[:, :], z[:, :], AX.X)
                    dve.drain()
                    dve.tensor_scalar(own[:, :], m[:, :], SEEN, None, ALU.is_lt)
                    dve.tensor_scalar(neg_max[:, :], m[:, :], -1.0, None, ALU.mult).then_inc(z_ready, 1)
                    dve.wait_ge(acc_made, (t * H + h) + 1)
                    dve.reciprocal(r[:, :], acc[:, DH:HC])
                    dve.tensor_scalar(y[:, 0:DH], V[:, bass.ds(t, 1), h, 0:DH].squeeze(1), own[:, 0:1], None, ALU.mult)
                    dve.tensor_scalar(own[:, :], own[:, :], -1.0, 1.0, ALU.mult, ALU.add)
                    dve.drain()
                    dve.tensor_tensor(out=r[:, :], in0=r[:, :], in1=own[:, :], op=ALU.mult)
                    dve.drain()
                    dve.scalar_tensor_tensor(out=agg[:, h * DH:(h + 1) * DH], in0=acc[:, 0:DH], scalar=r[:, 0:1],
                                             in1=y[:, 0:DH], op0=ALU.mult, op1=ALU.add).then_inc(acc_free, 1)
                    dve.drain()
                dve.tensor_scalar(ex[:, :], agg[:, :], 0.0, None, ALU.min).then_inc(low_made, 1)
                dve.wait_ge(ex_made, t + 1)
                dve.scalar_tensor_tensor(out=y[:, :], in0=agg[:, :], scalar=0.0, in1=ex[:, :], op0=ALU.max, op1=ALU.add)
                dve.drain()
                dve.wait_ge(x_loaded, t * 16 + 16)
                dve.scalar_tensor_tensor(out=y[:, :], in0=y[:, :], scalar=-1.0, in1=xin[:, :], op0=ALU.add, op1=ALU.add).then_inc(tile_done, 1)
                layernorm_dve(dve, y, out1, st, mv, var_made, rstd_made, t + 1)
                dve.drain()
                dve.tensor_tensor_reduce(out=ex[:, :], in0=out1[:, :], in1=sh.hv[:, :], scale=1.0, scalar=0.0,
                                         op0=ALU.mult, op1=ALU.add, accum_out=s1[:, 0:1])
                dve.drain()
                dve.tensor_copy(sh.S[:, bass.ds(t, 1)], s1[:, :]).then_inc(s_made, 1)
                dve.drain().then_inc(x1_made, 1)
                dve.wait_ge(x1_stored, t * 16 + 16)

        @block.gpsimd
        def _(pool):
            with pool.Fori(0, T) as t:
                rstd_pool(pool, sh, mv, var_made, rstd_made, t + 1)

        @block.scalar
        def _(act):
            act.sem_inc(pt_copied, 2)
            with act.Fori(0, T) as t:
                for h in range(H):
                    attend_act(act, z, neg_max, pt, ps_t, t * H + h, z_ready, z_made, zt_made, pt_copied, pt_used)
                act.wait_ge(low_made, t + 1)
                act.activation(ex[:, :], ex[:, :], ACT.Exp).then_inc(ex_made, 1)

        @block.tensor
        def _(pe):
            pe.sem_inc(pt_used, 2)
            with pe.Fori(0, T) as t:
                for h in range(H):
                    attend_pe(pe, sh, z, pt, ps_t, acc[:, :], t * H + h, lambda j: V[:, j, h, :],
                              z_made, zt_made, pt_copied, pt_used, acc_free, acc_made)


def general_layer1(nc, sh, adj, out):
    CH = 2048
    with ExitStack() as ctx:
        def sem(name):
            return ctx.enter_context(nc.semaphore(name))

        def sb(name, shape, dt=F32):
            return ctx.enter_context(nc.sbuf_tensor(name, shape, dt))

        X1 = sb("g1_x1", [P, T, D + 1])
        A = sb("g1_adj", [P, N])
        z = sb("g1_z", [P, N])
        sbc = sb("g1_s", [P, N])
        hide = sb("g1_hide", [P, CH])
        y, out1 = sb("g1_y", [P, D]), sb("g1_out", [P, D])
        pt = sb("g1_pt", [P, 2, GB * P])
        neg_max, m, seen, r = (sb(f"g1_{s}", [P, 1]) for s in ("nm", "m", "seen", "r"))
        st, mv = sb("g1_st", [P, 6]), sb("g1_mv", [P, 2])
        ps_t = [ctx.enter_context(nc.psum_tensor(f"g1_pst{i}", [P, GB * P], F32)) for i in range(2)]
        acc = ctx.enter_context(nc.psum_tensor("g1_acc", [P, D + 1], F32))
        x1_loaded, s_loaded, adj_loaded, adj_used = sem("g1_x1"), sem("g1_s_loaded"), sem("g1_adj_loaded"), sem("g1_adj_used")
        ones_made = sem("g1_ones")
        z_ready, z_made, zt_made, pt_copied = sem("g1_z_ready"), sem("g1_z_made"), sem("g1_zt_made"), sem("g1_pt_copied")
        pt_used, acc_free, acc_made = sem("g1_pt_used"), sem("g1_acc_free"), sem("g1_acc_made")
        var_made, rstd_made, y_made, y_stored = sem("g1_var"), sem("g1_rstd"), sem("g1_y_made"), sem("g1_y_stored")
        block = ctx.enter_context(nc.Block())

        @block.sync
        def _(sp):
            sp.dma_start(X1[:, :, 0:D], sh.x1_dram.rearrange("(t p) d -> p t d", p=P)).then_inc(x1_loaded, 16)
            sp.dma_start(sbc[:, :], sh.s_dram[0:1, :].to_broadcast([P, N])).then_inc(s_loaded, 16)
            with sp.Fori(0, T) as t:
                sp.wait_ge(adj_used, t + 1)
                sp.dma_start(A[:, :], adj[bass.ds(t * P, P), :]).then_inc(adj_loaded, 16)
                sp.wait_ge(y_made, t + 1)
                sp.dma_start(out[bass.ds(t * P, P), :], out1[:, :]).then_inc(y_stored, 16)
            sp.wait_ge(y_stored, 16 * T)

        @block.vector
        def _(dve):
            dve.sem_inc(adj_used, 1)
            dve.sem_inc(acc_free, 1)
            dve.wait_ge(s_loaded, 16)
            dve.wait_ge(x1_loaded, 16)
            with dve.Fori(0, T) as t:
                dve.wait_ge(adj_loaded, t * 16 + 16)
                dve.tensor_tensor(out=z[:, :], in0=A[:, :], in1=sbc[:, :], op=ALU.mult)
                for c in range(N // CH):
                    cs = slice(c * CH, (c + 1) * CH)
                    dve.drain()
                    dve.tensor_scalar(hide[:, :], A[:, cs], 0.0, HIDDEN, ALU.is_equal, ALU.mult)
                    dve.drain()
                    dve.tensor_tensor(out=z[:, cs], in0=z[:, cs], in1=hide[:, :], op=ALU.add)
                dve.drain().then_inc(adj_used, 1)
                dve.reduce_max(m[:, :], z[:, :], AX.X)
                dve.drain()
                dve.tensor_scalar(seen[:, :], m[:, :], SEEN, None, ALU.is_ge)
                dve.tensor_scalar(neg_max[:, :], m[:, :], -1.0, None, ALU.mult).then_inc(z_ready, 1)
                dve.wait_ge(acc_made, t + 1)
                dve.reciprocal(r[:, :], acc[:, D:D + 1])
                dve.drain()
                dve.tensor_tensor(out=r[:, :], in0=r[:, :], in1=seen[:, :], op=ALU.mult)
                dve.drain()
                dve.scalar_tensor_tensor(out=y[:, :], in0=acc[:, 0:D], scalar=r[:, 0:1],
                                         in1=X1[:, bass.ds(t, 1), 0:D].squeeze(1), op0=ALU.mult, op1=ALU.add).then_inc(acc_free, 1)
                layernorm_dve(dve, y, out1, st, mv, var_made, rstd_made, t + 1).then_inc(y_made, 1)
                dve.wait_ge(y_stored, t * 16 + 16)

        @block.gpsimd
        def _(pool):
            pool.memset(X1[:, :, D:D + 1], 1.0).then_inc(ones_made, 1)
            with pool.Fori(0, T) as t:
                rstd_pool(pool, sh, mv, var_made, rstd_made, t + 1)

        @block.scalar
        def _(act):
            act.sem_inc(pt_copied, 2)
            with act.Fori(0, T) as t:
                attend_act(act, z, neg_max, pt, ps_t, t, z_ready, z_made, zt_made, pt_copied, pt_used)

        @block.tensor
        def _(pe):
            pe.sem_inc(pt_used, 2)
            pe.wait_ge(ones_made, 1)
            pe.wait_ge(x1_loaded, 16)
            with pe.Fori(0, T) as t:
                attend_pe(pe, sh, z, pt, ps_t, acc[:, :], t, lambda j: X1[:, j, :],
                          z_made, zt_made, pt_copied, pt_used, acc_free, acc_made)


def general(nc, sh, x, adj, out):
    with nc.sbuf_tensor("V_general", [P, T, H, HC], F32) as V:
        with nc.semaphore("ones_in_v") as ones_in_v, nc.Block() as block:
            @block.gpsimd
            def _(pool):
                pool.memset(V[:, :, :, DH:HC], 1.0).then_inc(ones_in_v, 1)
                pool.wait_ge(ones_in_v, 1)
        project(nc, sh, V, x, "g_")
        general_layer0(nc, sh, V, x, adj)
    general_layer1(nc, sh, adj, out)


SUP = 512
NS = N // SUP
IT = SUP // P
CG = 8
NGR = T // CG
RING = 4
MXQ = 1024
NMX = IT * (N // MXQ)
Q = 4
QW = N // Q
LIMIT = 1.0e15
A_LIMIT = 1.0e30


def need(eng, sem, value):
    if not isinstance(value, int) or value > 0:
        eng.wait_ge(sem, value)


def gate(eng, sem, value, passed):
    if not isinstance(value, int):
        eng.wait_ge(sem, value)
        eng.sem_inc(passed, 1)
    else:
        need(eng, sem, value)


def load_adj_group(sp, R, adj, row, g):
    col = (g % NGR) * CG * P
    sp.dma_start(R.G[:, g % RING, :, :], adj[bass.ds(row, SUP), col:col + CG * P].rearrange("(t p) j -> p t j", p=P)
                 ).then_inc(R.group_loaded[g % RING], 16)


def factors(nc, sh, F, R, V, adj):
    with ExitStack() as ctx:
        def sem(name):
            return ctx.enter_context(nc.semaphore(name))

        part_max = ctx.enter_context(nc.sbuf_tensor("f_part_max", [P, H], F32))
        emax = ctx.enter_context(nc.sbuf_tensor("f_emax", [P, H], F32))
        rows = ctx.enter_context(nc.sbuf_tensor("f_rows", [T, H, P], F32))
        ps = ctx.enter_context(nc.psum_tensor("f_ps", [T, H, P], F32))
        part_made, emax_made, shifted, exp_made = sem("f_part"), sem("f_emax_made"), sem("f_shift"), sem("f_exp")
        rows_made, rows_copied, rows_stored, v_scaled = sem("f_rows_made"), sem("f_rows_copied"), sem("f_rows_stored"), sem("f_v")
        block = ctx.enter_context(nc.Block())

        def scale_v(eng, tiles):
            for t0 in tiles:
                eng.tensor_tensor(out=V[:, t0:t0 + 8, :, :].rearrange("p t h d -> p (t h) d"),
                                  in0=V[:, t0:t0 + 8, :, :].rearrange("p t h d -> p (t h) d"),
                                  in1=F.z[:, t0:t0 + 8, :].rearrange("p t h -> p (t h)").unsqueeze(2).to_broadcast([P, 8 * H, DH]),
                                  op=ALU.mult).then_inc(v_scaled, 1)

        @block.vector
        def _(dve):
            dve.tensor_reduce(part_max[:, :], sh.E[:, :, H:2 * H].rearrange("p t h -> p h t"), AX.X, ALU.max).then_inc(part_made, 1)
            dve.wait_ge(emax_made, 1)
            over = emax[:, :].unsqueeze(1).to_broadcast([P, T, H])
            dve.tensor_tensor(out=F.t[:, :, :], in0=sh.E[:, :, H:2 * H], in1=over, op=ALU.subtract)
            dve.tensor_tensor(out=F.a[:, :, :], in0=sh.E[:, :, 0:H], in1=over, op=ALU.add).then_inc(shifted, 1)
            dve.wait_ge(rows_made, 1)
            dve.tensor_copy(rows[:, :, :], ps[:, :, :]).then_inc(rows_copied, 1)
            scale_v(dve, range(0, T * 3 // 4, 8))

        @block.gpsimd
        def _(pool):
            pool.wait_ge(part_made, 1)
            pool.partition_all_reduce(emax[:, :], part_max[:, :], P, bass.bass_isa.ReduceOp.max).then_inc(emax_made, 1)
            pool.wait_ge(exp_made, 1)
            scale_v(pool, range(T * 3 // 4, T, 8))

        @block.scalar
        def _(act):
            act.wait_ge(shifted, 1)
            act.activation(F.z[:, :, :], F.t[:, :, :], ACT.Exp, scale=SLOPE).then_inc(exp_made, 1)
            act.activation(F.t[:, :, :], F.t[:, :, :], ACT.Exp, scale=1.0 - SLOPE).then_inc(exp_made, 1)
            act.activation(F.a[:, :, :], F.a[:, :, :], ACT.Exp, scale=1.0 - SLOPE).then_inc(exp_made, 1)

        @block.tensor
        def _(pe):
            pe.wait_ge(exp_made, 3)
            for h in range(H):
                last = pe.transpose(ps[:, h, :], F.a[:, :, h], sh.ident[:, :])
            last.then_inc(rows_made, 1)

        @block.sync
        def _(sp):
            load_adj_group(sp, R, adj, 0, 0)
            sp.wait_ge(rows_copied, 1)
            sp.dma_start(sh.a_dram.rearrange("h (t p) -> t h p", p=P), rows[:, :, :]).then_inc(rows_stored, 16)
            sp.wait_ge(rows_stored, 16)


class AdjRing:

    def __init__(self, nc, ctx):
        G = ctx.enter_context(nc.sbuf_tensor("adj_ring", [P, RING * IT * CG * P], F32))
        self.G = G[:, :].rearrange("p (r t j) -> p r t j", r=RING, t=IT)
        self.A = G[:, :].rearrange("p (b j) -> p b j", b=2)
        self.group_loaded = [ctx.enter_context(nc.semaphore(f"group_loaded{i}")) for i in range(RING)]
        self.quarter_loaded = [[ctx.enter_context(nc.semaphore(f"quarter_loaded{b}{q}")) for q in range(Q)] for b in range(2)]


class Factors:

    def __init__(self, nc, ctx):
        self.a, self.t, self.z, self.r = (
            ctx.enter_context(nc.sbuf_tensor(f"fac_{s}", [P, T, H], F32)) for s in "atzr")
        self.first_max = ctx.enter_context(nc.sbuf_tensor("fac_first_max", [P, T // 8, IT], F32))


def fast_layer0(nc, sh, F, R, V, x, adj):
    with ExitStack() as ctx:
        def sem(name):
            return ctx.enter_context(nc.semaphore("l0_" + name))

        def sb(name, shape, dt=F32):
            return ctx.enter_context(nc.sbuf_tensor("l0_" + name, shape, dt))

        G, adj_loaded = R.G, R.group_loaded
        hide = sb("hide", [P, 2, CG * P])
        mx_in = sb("mx_in", [P, 2, MXQ])
        ab = sb("ab", [P, H, SUP])
        W = sb("W", [P, RING, H, SUP])
        mx_part, mx4 = sb("mx_part", [P, NMX]), sb("mx4", [P, IT])
        nm_next, nm = sb("nm_next", [P, IT]), sb("nm", [P, IT])
        oT, dT = sb("oT", [P, 2, SUP]), sb("dT", [P, SUP])
        r4, mv = sb("r4", [P, 2, H]), sb("mv", [P, 2, 4])
        agg, ex = sb("agg", [P, 2, D]), sb("ex", [P, 2, D])
        xin = sh.E[:, :, :].rearrange("p (b t) f -> p b (t f)", b=2)
        y = sb("y", [P, 2, D])
        st, s1, eps = sb("st", [P, 6]), sb("s1", [P, 1]), sb("eps", [P, 1])
        gT = [ctx.enter_context(nc.psum_tensor(f"l0_gT{i}", [P, SUP], F32)) for i in range(RING)]
        acc = [ctx.enter_context(nc.psum_tensor(f"l0_acc{i}", [P, SUP], F32)) for i in range(2)]
        den = ctx.enter_context(nc.psum_tensor("l0_den", [P, SUP], F32))
        back = ctx.enter_context(nc.psum_tensor("l0_back", [P, D + P], F32))

        hide_made, hidden, g_made = sem("hide_made"), sem("hidden"), sem("g_made")
        gt_made, at_act, at_pool, w_made, mm_done = sem("gt_made"), sem("at_act"), sem("at_pool"), sem("w_made"), sem("mm_done")
        mx_loaded = [sem(f"mx_loaded{i}") for i in range(2)]
        mx_read, nm_made, nm_taken = sem("mx_read"), sem("nm_made"), sem("nm_taken")
        ab_loaded = [sem(f"ab_loaded{h}") for h in range(H)]
        ab_used, sums_copied, pool_passed = sem("ab_used"), sem("sums_copied"), sem("pool_passed")
        back_made, agg_made, low_made, ex_made = sem("back_made"), sem("agg_made"), sem("low_made"), sem("ex_made")
        y_made, mv_made, rstd_made, x1_made, s_made = sem("y_made"), sem("mv_made"), sem("rstd_made"), sem("x1_made"), sem("s_made")
        xin_loaded = [sem(f"xin_loaded{i}") for i in range(2)]
        x1_stored = [sem(f"x1_stored{i}") for i in range(2)]
        eps_made, sp_passed = sem("eps_made"), sem("sp_passed")
        block = ctx.enter_context(nc.Block())

        STEP = 11

        MAX_AT = [c for c in range(56) if c % 2 == 0 or c % 14 == 7]
        assert len(MAX_AT) == NMX

        def max_slot(c):
            return MAX_AT.index(c) if c in MAX_AT else None

        def when(c, start):
            return (c - start) // STEP if c >= start and (c - start) % STEP == 0 and (c - start) // STEP < IT else None

        @block.sync
        def _(sp):
            def load_group(s, g):
                gate(sp, gt_made, s * T + CG * (g - RING + 1), sp_passed)
                load_adj_group(sp, R, adj, (s + g // NGR) * SUP, g)

            def load_max(s, m):
                gate(sp, mx_read, (s - 1) * NMX + m + 1, sp_passed)
                it, q = m // (N // MXQ), m % (N // MXQ)
                sp.dma_start(mx_in[:, m % 2, :], adj[bass.ds(s * SUP + it * P, P), q * MXQ:(q + 1) * MXQ]).then_inc(mx_loaded[m % 2], 16)

            def load_ab(s):
                for h in range(H):
                    if h == H - 1:
                        gate(sp, at_pool, s * T, sp_passed)
                    elif h == H - 2:
                        gate(sp, at_act, s * T, sp_passed)
                    else:
                        gate(sp, ab_used, (s - 1) * (H - 2) + h + 1, sp_passed)
                    sp.dma_start(ab[:, h, :], sh.a_dram[h:h + 1, bass.ds(s * SUP, SUP)].to_broadcast([P, SUP])
                                 ).then_inc(ab_loaded[h], 16)

            def load_x(s, it):
                gate(sp, low_made, s * IT + it + 1, sp_passed)
                sp.dma_start(xin[:, it % 2, :], x[bass.ds(s * SUP + it * P, P), :]).then_inc(xin_loaded[it % 2], 16)

            def store_x1(s, it):
                gate(sp, x1_made, s * IT + it + 3, sp_passed)
                sp.dma_start(sh.x1_dram[bass.ds(s * SUP + it * P, P), :], y[:, it % 2, :]).then_inc(x1_stored[it % 2], 16)

            def body(s, first, last):
                for c in range(T):
                    if c % CG == 0 and not (last and c // CG + 3 >= NGR):
                        load_group(s, c // CG + 3)
                    if max_slot(c) is not None and not last:
                        load_max(s + 1, max_slot(c))
                    if when(c, 1) is not None and not first:
                        load_x(s - 1, when(c, 1))
                    if when(c, 28) is not None and not first:
                        store_x1(s - 1, when(c, 28))
                    if c == T - CG and last:
                        sp.wait_ge(gt_made, s * T + c - CG)
                        for q in range(Q):
                            sp.dma_start(R.A[:, 0, q * QW:(q + 1) * QW], adj[0:P, q * QW:(q + 1) * QW]
                                         ).then_inc(R.quarter_loaded[0][q], 16)
                if not last:
                    load_ab(s + 1)

            for i in range(2):
                sp.sem_inc(x1_stored[i], 16)
            load_ab(0)
            load_group(0, 1)
            load_group(0, 2)
            body(0, True, False)
            with sp.Fori(1, NS - 1) as s:
                body(s, False, False)
            body(NS - 1, False, True)
            for it in range(IT):
                load_x(NS - 1, it)
                if it >= 1:
                    store_x1(NS - 1, it - 1)
            store_x1(NS - 1, IT - 1)
            for i in range(2):
                sp.wait_ge(x1_stored[i], 16 * T // 2 + 16)

        @block.vector
        def _(dve):
            def weigh(s, c):
                need(dve, at_act, s * T + (c + 1))
                need(dve, at_pool, s * T + (c + 1))
                need(dve, gt_made, s * T + (c + 1))
                w = W[:, c % RING, :, :]
                dve.scalar_tensor_tensor(out=w, in0=w, scalar=1.0,
                                         in1=gT[c % RING][:, :].unsqueeze(1).to_broadcast([P, H, SUP]),
                                         op0=ALU.max, op1=ALU.mult).then_inc(w_made, 1)

            def hide_zeros(s, g, it):
                n = s * (NGR * IT) + (g * IT + it)
                need(dve, adj_loaded[g % RING], s * 32 + 16 * (g // RING + 1))
                need(dve, hidden, n - 1)
                dve.tensor_scalar(hide[:, it % 2, :], G[:, g % RING, it, :], 0.0, HIDDEN,
                                  ALU.is_equal, ALU.mult).then_inc(hide_made, 1)

            def row_max(s, m):
                need(dve, mx_loaded[m % 2], (s - 1) * (NMX * 8) + 16 * (m // 2 + 1))
                dve.reduce_max(mx_part[:, m:m + 1], mx_in[:, m % 2, :], AX.X).then_inc(mx_read, 1)

            def finish_max(s, parts):
                dve.drain()
                dve.tensor_reduce(mx4[:, :], parts, AX.X, ALU.max)
                dve.drain()
                need(dve, nm_taken, s)
                dve.tensor_scalar(nm_next[:, :], mx4[:, :], 0.0, -1.0, ALU.max, ALU.mult).then_inc(nm_made, 1)

            def normalise(s, it):
                e = s * IT + it
                need(dve, back_made, e + 2)
                need(dve, low_made, e + 1)
                dve.reciprocal(r4[:, it % 2, :], back[:, D:D + P:P // H])
                dve.drain()
                dve.tensor_tensor(out=agg[:, it % 2, :].rearrange("p (h d) -> p h d", h=H),
                                  in0=back[:, 0:D].rearrange("p (h d) -> p h d", h=H),
                                  in1=r4[:, it % 2, :].unsqueeze(2).to_broadcast([P, H, DH]), op=ALU.mult).then_inc(agg_made, 1)

            def stats(s, it):
                e = s * IT + it
                need(dve, x1_made, e + 1)
                need(dve, y_made, e + 1)
                dve.bn_stats(st[:, :], y[:, it % 2, :])
                dve.drain()
                dve.bn_aggr(mv[:, it % 2, 0:2], st[:, :]).then_inc(mv_made, 1)

            def score(s, it):
                need(dve, x1_made, s * IT + it + 3)
                dve.tensor_tensor_reduce(out=ex[:, it % 2, :], in0=y[:, it % 2, :], in1=sh.hv[:, :], scale=1.0, scalar=0.0,
                                         op0=ALU.mult, op1=ALU.add, accum_out=s1[:, 0:1])
                dve.drain()
                dve.tensor_copy(sh.S[:, bass.ds(s * IT + it, 1)], s1[:, :]).then_inc(s_made, 1)

            def body(s, first, last):
                for c in range(T):
                    weigh(s, c)
                    g = c // CG + 2
                    if c % 2 == 1 and not (last and g >= NGR):
                        hide_zeros(s, g, c % CG // 2)
                    if max_slot(c) is not None and not last:
                        row_max(s + 1, max_slot(c))
                    if c == 55 and not last:
                        finish_max(s + 1, mx_part[:, :].rearrange("p (t q) -> p t q", t=IT))
                    if not first:
                        for start, step in ((7, normalise), (17, stats), (24, score)):
                            if when(c, start) is not None:
                                step(s - 1, when(c, start))

            dve.sem_inc(mx_read, 2)
            dve.sem_inc(agg_made, 1)
            dve.sem_inc(s_made, 2)
            finish_max(0, F.first_max[:, :, :].rearrange("p u t -> p t u"))
            for it in range(IT):
                hide_zeros(0, 0, it)
            for it in range(IT):
                hide_zeros(0, 1, it)
            body(0, True, False)
            with dve.Fori(1, NS - 1) as s:
                body(s, False, False)
            body(NS - 1, False, True)
            for it in range(IT + 1):
                if it < IT:
                    normalise(NS - 1, it)
                if it >= 1:
                    stats(NS - 1, it - 1)
                    score(NS - 1, it - 1)

        @block.gpsimd
        def _(pool):
            def outer(s, c):
                if c == 0:
                    need(pool, ab_loaded[H - 1], s * 16 + 16)
                gate(pool, mm_done, s * T + (c - RING + 1), pool_passed)
                pool.tensor_scalar(W[:, c % RING, H - 1, :], ab[:, H - 1, :], F.t[:, c, H - 1:H], 0.0,
                                   ALU.mult, ALU.add).then_inc(at_pool, 1)

            def hide_add(s, g, it):
                n = s * (NGR * IT) + (g * IT + it)
                need(pool, hide_made, n + 1)
                pool.tensor_tensor(out=G[:, g % RING, it, :], in0=G[:, g % RING, it, :], in1=hide[:, it % 2, :],
                                   op=ALU.add).then_inc(hidden, 1)

            def elu_parts(s, it):
                e, b = s * IT + it, it % 2
                need(pool, x1_stored[b], s * 32 + 16 * (it // 2 + 1))
                need(pool, s_made, e + 1)
                need(pool, xin_loaded[b], s * 32 + 16 * (it // 2 + 1))
                gate(pool, agg_made, e + 2, pool_passed)
                pool.tensor_copy(F.r[:, bass.ds(e, 1), :].squeeze(1), r4[:, b, :])
                pool.tensor_scalar(ex[:, b, :], agg[:, b, :], 0.0, -3.0e38, ALU.min, ALU.max)
                pool.tensor_scalar(agg[:, b, :], agg[:, b, :], 3.0e38, 0.0, ALU.min, ALU.max)
                pool.drain()
                pool.tensor_tensor(out=y[:, b, :], in0=agg[:, b, :], in1=xin[:, b, :], op=ALU.add).then_inc(low_made, 1)

            def residual(s, it):
                b = it % 2
                gate(pool, ex_made, s * IT + it + 1, pool_passed)
                pool.tensor_scalar(ex[:, b, :], ex[:, b, :], -1.0, 1.0, ALU.add, ALU.mult)
                pool.drain()
                pool.tensor_tensor(out=y[:, b, :], in0=y[:, b, :], in1=ex[:, b, :], op=ALU.add).then_inc(y_made, 1)

            def rstd(s, it):
                b = it % 2
                need(pool, mv_made, s * IT + it + 1)
                pool.tensor_tensor(out=mv[:, b, 1:2], in0=mv[:, b, 1:2], in1=eps[:, :], op=ALU.add)
                pool.drain()
                pool.tensor_tensor(out=mv[:, b, 2:3], in0=mv[:, b, 1:2], in1=sh.neg_half[:, :], op=ALU.pow)
                pool.drain()
                pool.tensor_tensor(out=mv[:, b, 3:4], in0=mv[:, b, 0:1], in1=mv[:, b, 2:3], op=ALU.mult)
                pool.drain()
                pool.tensor_scalar(mv[:, b, 3:4], mv[:, b, 3:4], -1.0, 0.0, ALU.mult, ALU.add).then_inc(rstd_made, 1)

            def body(s, first, last):
                for c in range(T):
                    outer(s, c)
                    g = (c + 2) // CG + 1
                    if c % 2 == 0 and not (last and g >= NGR):
                        hide_add(s, g, (c + 2) % CG // 2)
                    if not first:
                        for start, step in ((13, elu_parts), (19, residual), (23, rstd)):
                            if when(c, start) is not None:
                                step(s - 1, when(c, start))

            pool.sem_inc(low_made, 2)
            pool.memset(eps[:, :], EPS).then_inc(eps_made, 1)
            for it in range(IT):
                hide_add(0, 0, it)
            hide_add(0, 1, 0)
            body(0, True, False)
            with pool.Fori(1, NS - 1) as s:
                body(s, False, False)
            body(NS - 1, False, True)
            for it in range(IT + 1):
                if it < IT:
                    elu_parts(NS - 1, it)
                if it >= 1:
                    residual(NS - 1, it - 1)
                    rstd(NS - 1, it - 1)

        @block.scalar
        def _(act):
            def outer(s, c):
                need(act, mm_done, s * T + (c - RING + 1))
                for h in range(H - 1):
                    if c == 0:
                        need(act, ab_loaded[h], s * 16 + 16)
                    last = act.activation(W[:, c % RING, h, :], ab[:, h, :], ACT.Copy, scale=F.t[:, c, h:h + 1])
                    if c == T - 1 and h < H - 2:
                        last.then_inc(ab_used, 1)
                last.then_inc(at_act, 1)

            def exponentiate(s, g, it):
                n = s * (NGR * IT) + (g * IT + it)
                need(act, hidden, n + 1)
                act.activation(G[:, g % RING, it, :], G[:, g % RING, it, :], ACT.Exp, bias=nm[:, it:it + 1], scale=1.0
                               ).then_inc(g_made, 1)

            def take_max(s):
                need(act, g_made, s * (NGR * IT))
                need(act, nm_made, s + 1)
                act.activation(nm[:, :], nm_next[:, :], ACT.Copy).then_inc(nm_taken, 1)
                act.drain()

            def copy_sums(s):
                need(act, mm_done, s * T + T)
                need(act, back_made, s * IT + 1)
                for q in range(2):
                    act.activation(oT[:, q, :], acc[q][:, :], ACT.Copy)
                act.activation(dT[:, :], den[:, :], ACT.Copy).then_inc(sums_copied, 1)

            def elu_exp(s, it):
                need(act, low_made, s * IT + it + 3)
                act.activation(ex[:, it % 2, :], ex[:, it % 2, :], ACT.Exp).then_inc(ex_made, 1)

            def norm(s, it):
                b = it % 2
                need(act, rstd_made, s * IT + it + 1)
                act.activation(y[:, b, :], y[:, b, :], ACT.Identity, bias=mv[:, b, 3:4], scale=mv[:, b, 2:3]
                               ).then_inc(x1_made, 1)

            def body(s, first, last):
                for c in range(T):
                    if c == RING - 1 and not first:
                        copy_sums(s - 1)
                    outer(s, c)
                    g = c // CG + 1
                    if c == T - 5 and not last:
                        take_max(s + 1)
                    if c % CG >= CG - IT and not (last and g >= NGR):
                        exponentiate(s, g, c % CG - (CG - IT))
                    if not first:
                        for start, step in ((15, elu_exp), (25, norm)):
                            if when(c, start) is not None:
                                step(s - 1, when(c, start))

            act.sem_inc(x1_made, 2)
            take_max(0)
            for it in range(IT):
                exponentiate(0, 0, it)
            body(0, True, False)
            with act.Fori(1, NS - 1) as s:
                body(s, False, False)
            body(NS - 1, False, True)
            copy_sums(NS - 1)
            for it in range(IT + 1):
                if it < IT:
                    elu_exp(NS - 1, it)
                if it >= 1:
                    norm(NS - 1, it - 1)

        @block.tensor
        def _(pe):
            def turn(s, c):
                if c % CG == 0:
                    need(pe, g_made, s * (NGR * IT) + (c // CG + 1) * IT)
                need(pe, w_made, s * T + (c - RING + 1))
                for it in range(IT):
                    last = pe.transpose(gT[c % RING][:, it * P:(it + 1) * P],
                                        G[:, c // CG % RING, it, (c % CG) * P:(c % CG + 1) * P], sh.ident[:, :])
                last.then_inc(gt_made, 1)

            def turn_ahead(s, c, last):
                if c < T:
                    turn(s, c)
                elif not last:
                    turn(s + 1, c - T)

            def product(s, c):
                if c == 0:
                    need(pe, sums_copied, s)
                need(pe, w_made, s * T + (c + 1))
                for h in range(H):
                    half = slice(h % 2 * DH, h % 2 * DH + DH)
                    pe.matmul(acc[h // 2][half, :], V[:, c, h, :], W[:, c % RING, h, :], start=(c == 0), stop=(c == T - 1))
                for h in range(H):
                    last = pe.matmul(den[h * 32:(h + 1) * 32, :], F.z[:, c, h:h + 1].to_broadcast([P, 32]),
                                     W[:, c % RING, h, :], start=(c == 0), stop=(c == T - 1))
                last.then_inc(mm_done, 1)

            def turn_back(s, it):
                e = s * IT + it
                if it == 0:
                    need(pe, sums_copied, s + 1)
                need(pe, agg_made, e + 1)
                for q in range(2):
                    pe.transpose(back[:, q * P:(q + 1) * P], oT[:, q, it * P:(it + 1) * P], sh.ident[:, :])
                pe.transpose(back[:, D:D + P], dT[:, it * P:(it + 1) * P], sh.ident[:, :]).then_inc(back_made, 1)

            def body(s, first, last):
                for c in range(T):
                    turn_ahead(s, c + 3, last)
                    if when(c, 4) is not None and not first:
                        turn_back(s - 1, when(c, 4))
                    product(s, c)

            pe.sem_inc(back_made, 1)
            for c in range(3):
                turn(0, c)
            body(0, True, False)
            with pe.Fori(1, NS - 1) as s:
                body(s, False, False)
            body(NS - 1, False, True)
            for it in range(IT):
                turn_back(NS - 1, it)


def score_rows(nc, sh, F, ok):
    with ExitStack() as ctx:
        def sem(name):
            return ctx.enter_context(nc.semaphore(name))

        row = ctx.enter_context(nc.sbuf_tensor("sr_row", [T, P], F32))
        fine = ctx.enter_context(nc.sbuf_tensor("sr_fine", [P, 2, T * H], F32))
        ps = ctx.enter_context(nc.psum_tensor("sr_ps", [T, P], F32))
        turned, copied, stored = sem("sr_turned"), sem("sr_copied"), sem("sr_stored")
        block = ctx.enter_context(nc.Block())

        @block.tensor
        def _(pe):
            pe.transpose(ps[:, :], sh.S[:, :], sh.ident[:, :]).then_inc(turned, 1)

        @block.vector
        def _(dve):
            dve.wait_ge(turned, 1)
            dve.tensor_copy(row[:, :], ps[:, :]).then_inc(copied, 1)
            a, r = F.a[:, :, :].rearrange("p t h -> p (t h)"), F.r[:, :, :].rearrange("p t h -> p (t h)")
            dve.scalar_tensor_tensor(out=fine[:, 0, :], in0=a, scalar=1.0, in1=r, op0=ALU.max, op1=ALU.mult)
            dve.tensor_scalar(fine[:, 1, :], a, A_LIMIT, None, ALU.is_le)
            dve.drain()
            dve.tensor_scalar(fine[:, 0, :], fine[:, 0, :], LIMIT, None, ALU.is_le)
            dve.drain()
            dve.tensor_tensor(out=fine[:, 0, :], in0=fine[:, 0, :], in1=fine[:, 1, :], op=ALU.mult)
            dve.drain()
            dve.tensor_reduce(ok[:, 0:1], fine[:, 0, :], AX.X, ALU.min)

        @block.sync
        def _(sp):
            sp.wait_ge(copied, 1)
            sp.dma_start(sh.s_dram[0, :].rearrange("(t p) -> t p", p=P), row[:, :]).then_inc(stored, 16)
            sp.wait_ge(stored, 16)


def fast_layer1(nc, sh, R, R1, adj, out):
    QG = NG // Q
    with ExitStack() as ctx:
        def sem(name):
            return ctx.enter_context(nc.semaphore("l1_" + name))

        def sb(name, shape, dt=F32):
            return ctx.enter_context(nc.sbuf_tensor("l1_" + name, shape, dt))

        X1 = sb("x1", [P, T, D])
        sbc = sb("sbc", [P, N])
        A, adj_loaded = R.A, R.quarter_loaded
        hide = sb("hide", [P, 2, QW])
        pt = sb("pt", [P, RING, GB * P])
        mq, nm, d4 = sb("mq", [P, 2, Q]), sb("nm", [P, 2, 1]), sb("d4", [P, 2, Q])
        y, out1 = sb("y", [P, 2, D]), sb("out", [P, 2, D])
        st, mv, r, eps = sb("st", [P, 6]), sb("mv", [P, 2, 4]), sb("r", [P, 1]), sb("eps", [P, 1])
        pT = [ctx.enter_context(nc.psum_tensor(f"l1_pT{i}", [P, GB * P], F32)) for i in range(RING)]
        acc = [ctx.enter_context(nc.psum_tensor(f"l1_acc{i}", [P, D], F32)) for i in range(2)]
        x1_loaded = [sem(f"x1_loaded{q}") for q in range(Q)]
        s_loaded = [sem(f"s_loaded{q}") for q in range(Q)]
        eps_made, sp_passed = sem("eps_made"), sem("sp_passed")
        hide_made, z_made, hidden, nm_made, p_made = sem("hide_made"), sem("z_made"), sem("hidden"), sem("nm_made"), sem("p_made")
        pT_made, pt_copied, mm_done, acc_read = sem("pT_made"), sem("pt_copied"), sem("mm_done"), sem("acc_read")
        mv_made, rstd_made, y_made = sem("mv_made"), sem("rstd_made"), sem("y_made")
        stored = [sem(f"stored{b}") for b in range(2)]
        block = ctx.enter_context(nc.Block())

        def pairs(eng, body):
            for b in range(2):
                body(b, b, False)
            with eng.Fori(1, T // 2 - 1) as u:
                for b in range(2):
                    body(u * 2 + b, b, False)
            for b in range(2):
                body(T - 2 + b, b, b == 1)

        @block.sync
        def _(sp):
            def load(t, b):
                for q in range(Q):
                    gate(sp, pT_made, (t - 2) * NG + QG * (q + 1), sp_passed)
                    sp.dma_start(A[:, b, q * QW:(q + 1) * QW], adj[bass.ds(t * P, P), q * QW:(q + 1) * QW]
                                 ).then_inc(adj_loaded[b][q], 16)

            def store(t, b):
                gate(sp, y_made, t + 1, sp_passed)
                sp.dma_start(out[bass.ds(t * P, P), :], out1[:, b, :]).then_inc(stored[b], 16)

            for b in range(2):
                sp.sem_inc(stored[b], 16)
            for q in range(Q):
                sp.dma_start(sbc[:, q * QW:(q + 1) * QW], sh.s_dram[0:1, q * QW:(q + 1) * QW].to_broadcast([P, QW])
                             ).then_inc(s_loaded[q], 16)
            for q in range(Q):
                tiles = slice(q * T // Q, (q + 1) * T // Q)
                sp.dma_start(X1[:, tiles, :], sh.x1_dram.rearrange("(t p) d -> p t d", p=P)[:, tiles, :]).then_inc(x1_loaded[q], 16)
            load(1, 1)
            load(2, 0)
            with sp.Fori(0, T // 2 - 2) as u:
                for b in range(2):
                    store(u * 2 + b, b)
                    load(u * 2 + (b + 3), 1 - b)
            store(T - 4, 0)
            load(T - 1, 1)
            for t in range(T - 3, T):
                store(t, t % 2)
            for b in range(2):
                sp.wait_ge(stored[b], 16 * T // 2 + 16)

        @block.vector
        def _(dve):
            def logits(t, b, last):
                for q in range(Q):
                    part = A[:, b, q * QW:(q + 1) * QW]
                    n = t * Q + q
                    need(dve, adj_loaded[b][q], (t - b) * 8 + 16)
                    need(dve, hidden, n - 1)
                    dve.tensor_scalar(hide[:, q % 2, :], part, 0.0, HIDDEN, ALU.is_equal, ALU.mult).then_inc(hide_made, 1)
                    if isinstance(t, int) and t == 0:
                        need(dve, s_loaded[q], 16)
                    dve.tensor_tensor_reduce(out=part, in0=part, in1=sbc[:, q * QW:(q + 1) * QW], scale=1.0, scalar=0.0,
                                             op0=ALU.mult, op1=ALU.max, accum_out=mq[:, b, q:q + 1]).then_inc(z_made, 1)
                dve.drain()
                need(dve, p_made, (t - 1) * Q)
                dve.tensor_reduce(nm[:, b, :], mq[:, b, :], AX.X, ALU.max, negate=True).then_inc(nm_made, 1)

            def finish(t, b):
                if isinstance(t, int) and t == 0:
                    for q in range(Q):
                        dve.wait_ge(x1_loaded[q], 16)
                need(dve, mm_done, t * NG + NG)
                dve.tensor_reduce(r[:, :], d4[:, b, :], AX.X, ALU.add)
                dve.drain()
                dve.reciprocal(r[:, :], r[:, :])
                dve.drain()
                dve.tensor_copy(R1[:, bass.ds(t, 1)], r[:, :])
                need(dve, y_made, t - 1)
                dve.scalar_tensor_tensor(out=y[:, b, :], in0=acc[b][:, :], scalar=r[:, 0:1],
                                         in1=X1[:, bass.ds(t, 1), :].squeeze(1), op0=ALU.mult, op1=ALU.add).then_inc(acc_read, 1)
                dve.drain()
                dve.bn_stats(st[:, :], y[:, b, :])
                dve.drain()
                dve.bn_aggr(mv[:, b, 0:2], st[:, :]).then_inc(mv_made, 1)

            def body(t, b, last):
                if not last:
                    logits(t + 1, 1 - b, last)
                finish(t, b)

            logits(0, 0, False)
            pairs(dve, body)

        @block.gpsimd
        def _(pool):
            def hide_add(t, b):
                for q in range(Q):
                    part = A[:, b, q * QW:(q + 1) * QW]
                    need(pool, z_made, t * Q + (q + 1))
                    pool.tensor_tensor(out=part, in0=part, in1=hide[:, q % 2, :], op=ALU.add).then_inc(hidden, 1)

            def rstd(t, b):
                need(pool, mv_made, t + 1)
                pool.tensor_tensor(out=mv[:, b, 1:2], in0=mv[:, b, 1:2], in1=eps[:, :], op=ALU.add)
                pool.drain()
                pool.tensor_tensor(out=mv[:, b, 2:3], in0=mv[:, b, 1:2], in1=sh.neg_half[:, :], op=ALU.pow)
                pool.drain()
                pool.tensor_tensor(out=mv[:, b, 3:4], in0=mv[:, b, 0:1], in1=mv[:, b, 2:3], op=ALU.mult)
                pool.drain()
                pool.tensor_scalar(mv[:, b, 3:4], mv[:, b, 3:4], -1.0, 0.0, ALU.mult, ALU.add).then_inc(rstd_made, 1)

            def body(t, b, last):
                if not last:
                    hide_add(t + 1, 1 - b)
                rstd(t, b)

            pool.memset(eps[:, :], EPS).then_inc(eps_made, 1)
            hide_add(0, 0)
            pairs(pool, body)

        @block.scalar
        def _(act):
            def probabilities(t, b, q):
                n = t * Q + q
                part = A[:, b, q * QW:(q + 1) * QW]
                if q == 0:
                    need(act, nm_made, t + 1)
                    need(act, acc_read, t - 1)
                need(act, hidden, n + 1)
                act.activation(part, part, ACT.Exp, bias=nm[:, b, :], scale=1.0, accum_out=d4[:, b, q:q + 1]).then_inc(p_made, 1)

            def norm(t, b):
                need(act, stored[b], (t - b) * 8 + 16)
                need(act, rstd_made, t + 1)
                act.activation(out1[:, b, :], y[:, b, :], ACT.Identity, bias=mv[:, b, 3:4], scale=mv[:, b, 2:3]).then_inc(y_made, 1)

            def body(t, b, last):
                for g in range(NG):
                    need(act, pT_made, t * NG + (g + 1))
                    need(act, mm_done, t * NG + (g - RING + 1))
                    act.activation(pt[:, g % RING, :], pT[g % RING][:, :], ACT.Copy).then_inc(pt_copied, 1)
                    if g == 5 and not (isinstance(t, int) and t == 0):
                        norm(t - 1, 1 - b)
                    if g >= NG - Q and not last:
                        probabilities(t + 1, 1 - b, g - (NG - Q))
                if last:
                    norm(t, b)

            for q in range(Q):
                probabilities(0, 0, q)
            pairs(act, body)

        @block.tensor
        def _(pe):
            def turn(t, b, g):
                if g % QG == 0:
                    need(pe, p_made, t * Q + (g // QG + 1))
                need(pe, pt_copied, t * NG + (g - RING + 1))
                for k in range(GB):
                    j = g * GB + k
                    last = pe.transpose(pT[g % RING][:, k * P:(k + 1) * P], A[:, b, j * P:(j + 1) * P], sh.ident[:, :])
                last.then_inc(pT_made, 1)

            def body(t, b, last):
                for g in range(NG):
                    if g + 3 < NG:
                        turn(t, b, g + 3)
                    elif not last:
                        turn(t + 1, 1 - b, g + 3 - NG)
                    need(pe, pt_copied, t * NG + (g + 1))
                    if g % QG == 0 and isinstance(t, int) and t == 0:
                        pe.wait_ge(x1_loaded[g // QG], 16)
                    if g == 0:
                        need(pe, acc_read, t - 1)
                    for k in range(GB):
                        j = g * GB + k
                        mm = pe.matmul(acc[b][:, :], pt[:, g % RING, k * P:(k + 1) * P], X1[:, j, :],
                                       start=(j == 0), stop=(j == T - 1))
                    mm.then_inc(mm_done, 1)

            for g in range(3):
                turn(0, 0, g)
            pairs(pe, body)


def verdict(nc, ok, R1, bad):
    with ExitStack() as ctx:
        def sem(name):
            return ctx.enter_context(nc.semaphore(name))

        fine = ctx.enter_context(nc.sbuf_tensor("v_fine", [P, T], F32))
        both = ctx.enter_context(nc.sbuf_tensor("v_both", [P, 2], F32))
        per_part, reduced = sem("v_part"), sem("v_reduced")
        block = ctx.enter_context(nc.Block())

        @block.vector
        def _(dve):
            dve.tensor_scalar(fine[:, :], R1[:, :], LIMIT, None, ALU.is_le)
            dve.drain()
            dve.tensor_reduce(both[:, 0:1], fine[:, :], AX.X, ALU.min)
            dve.drain()
            dve.tensor_tensor(out=both[:, 0:1], in0=both[:, 0:1], in1=ok[:, 0:1], op=ALU.mult)
            dve.drain()
            dve.tensor_scalar(both[:, 0:1], both[:, 0:1], -1.0, 1.0, ALU.mult, ALU.add).then_inc(per_part, 1)
            dve.wait_ge(reduced, 1)
            dve.tensor_copy(bad[:, 0:1], both[:, 1:2])

        @block.gpsimd
        def _(pool):
            pool.wait_ge(per_part, 1)
            pool.partition_all_reduce(both[:, 1:2], both[:, 0:1], P, bass.bass_isa.ReduceOp.max).then_inc(reduced, 1)


def program(nc, x, adj, W, a, hv, out):
    with ExitStack() as ctx:
        sh = Shared(nc, ctx)
        ok = ctx.enter_context(nc.sbuf_tensor("ok", [P, 1], F32))
        R1 = ctx.enter_context(nc.sbuf_tensor("R1", [P, T], F32))
        bad = ctx.enter_context(nc.sbuf_tensor("bad", [P, 1], I32))
        setup(nc, sh, W, a, hv)
        with ExitStack() as fast:
            R = AdjRing(nc, fast)
            with ExitStack() as layer0:
                F = Factors(nc, layer0)
                with nc.sbuf_tensor("V", [P, T, H, DH], F32) as V:
                    project(nc, sh, V, x, "f_", adj, F.first_max)
                    factors(nc, sh, F, R, V, adj)
                    fast_layer0(nc, sh, F, R, V, x, adj)
                score_rows(nc, sh, F, ok)
            fast_layer1(nc, sh, R, R1, adj, out)
        verdict(nc, ok, R1, bad)
        failed = nc.alloc_registers("guard_failed", engines=mybir.ALL_ENGINES)
        nc.regs_load(failed, bad[0:1, 0:1])
        nc.br_ne(failed, 0, on_true="general_path", on_false="program_end", engines=mybir.ALL_ENGINES)
        with nc.body("general_path", valid_engines=mybir.ALL_ENGINES):
            general(nc, sh, x, adj, out)
            nc.br("program_end", engines=mybir.ALL_ENGINES)
        nc.switch_bb("program_end")


_INS = ['x', 'adj', 'L0_gnn_W', 'L0_gnn_a', 'L1_gnn_H_v']
_OUTS = [((N, D), 'float32')]


def kernel(**inputs):
    import numpy as _np
    import concourse.bacc as _bacc
    from concourse import mybir as _mybir
    from concourse.bass_utils import run_bass_kernel_spmd as _run

    nc = _bacc.Bacc("TRN2", target_bir_lowering=False, num_devices=1)
    arrays, args = {}, []
    for name in _INS:
        a = _np.ascontiguousarray(inputs[name])
        arrays[f"in_{name}_dram"] = a
        args.append(nc.dram_tensor(f"in_{name}_dram", a.shape, _mybir.dt.from_np(a.dtype), kind="ExternalInput").ap())
    for i, (shape, dtype) in enumerate(_OUTS):
        dt = _mybir.dt.from_np(_np.dtype(dtype))
        args.append(nc.dram_tensor(f"out_{i}_dram", shape, dt, kind="ExternalOutput").ap())
    program(nc, *args)
    r = _run(nc, [arrays], core_ids=[0])
    return r.results[0]["out_0_dram"]
```
